# Optimizing a Trainium2 kernel written in Bass

```python
import numpy as np
import jax
import jax.numpy as jnp

def _softmax(x, axis=-1):
    return jax.nn.softmax(x, axis=axis)

def _gelu(x):
    return jax.nn.gelu(x, approximate=True)

def _silu(x):
    return jax.nn.silu(x)

def _sigmoid(x):
    return jax.nn.sigmoid(x)

def _layernorm(x, axis=-1, eps=1e-05):
    m = jnp.mean(x, axis=axis, keepdims=True)
    v = jnp.var(x, axis=axis, keepdims=True)
    return (x - m) / jnp.sqrt(v + eps)

def _scatter_add(tgt, idx, src, axis=0):
    return tgt.at[idx].add(src)

def _segment_sum(src, seg, n):
    return jax.ops.segment_sum(src, seg, n)
kernel_name = 'mk_cond_resid_d2_seqx_r4_4a8c89'

def setup_inputs(seed: int=0):
    np.random.seed(seed)
    _w = jnp.asarray

    def _rec_inputs():
        import jax
        import jax.numpy as jnp
        _rk = jax.random.key(seed)
        x = -7.109e-05 + 0.9999 * jax.random.normal(jax.random.fold_in(_rk, 1), (128, 64, 512), jnp.float32)
        _lenS = 64 - jax.random.randint(jax.random.fold_in(_rk, 7), (128,), 0, max(1, 64 // 4) + 1, jnp.int32)
        _lenS2 = 64 - jax.random.randint(jax.random.fold_in(_rk, 8), (128,), 0, max(1, 64 // 4) + 1, jnp.int32)
        itok_B_0_7 = jax.random.randint(jax.random.fold_in(_rk, 11), (128,), 0, 8, jnp.int32)
        itok_B_1_198 = jax.random.randint(jax.random.fold_in(_rk, 12), (128,), 1, 199, jnp.int32)
        return (x, itok_B_0_7, itok_B_1_198)
    x, itok_B_0_7, itok_B_1_198 = _rec_inputs()

    def _L0_cond_setup():
        import jax, jax.numpy as jnp
        import numpy as np
        B, C, D, T, N_SUBJECTS = (128, 64, 64, 512, 8)
        key = jax.random.key(seed)
        kx, ks, kw = jax.random.split(key, 3)
        x = jax.random.normal(kx, (B, C, T), dtype=jnp.float32)
        subjects = jax.random.randint(ks, (B,), 0, N_SUBJECTS, dtype=jnp.int64)
        weights = jax.random.normal(kw, (N_SUBJECTS, C, D), dtype=jnp.float32) * (1.0 / C ** 0.5)
        return {'x': x, 'subjects': subjects, 'weights': weights}
    _L0_cond_all = _L0_cond_setup()
    _L0_cond_in = {k: v for k, v in _L0_cond_all.items() if k in ('weights',)}
    del _L0_cond_all

    def _L1_cond_setup():
        import jax, jax.numpy as jnp
        import numpy as np
        B, C, T = (128, 64, 512)
        S, D = (200, 64)
        key = jax.random.key(seed)
        k1, k2, k3 = jax.random.split(key, 3)
        x = jax.random.normal(k1, (B, C, T), dtype=jnp.float32)
        conditions = jax.random.randint(k2, (B,), 0, S, dtype=jnp.int64)
        weights = jax.random.normal(k3, (S, C, D), dtype=jnp.float32) / jnp.sqrt(jnp.float32(C))
        return {'x': x, 'conditions': conditions, 'weights': weights}
    _L1_cond_all = _L1_cond_setup()
    _L1_cond_in = {k: v for k, v in _L1_cond_all.items() if k in ('weights',)}
    del _L1_cond_all
    return {'x': x, 'itok_B_0_7': itok_B_0_7, 'itok_B_1_198': itok_B_1_198, 'L0_cond_weights': _L0_cond_in['weights'], 'L1_cond_weights': _L1_cond_in['weights']}

def reference(x, itok_B_0_7, itok_B_1_198, L0_cond_weights, L1_cond_weights):
    import jax
    import jax.numpy as jnp

    def _L0_cond_ref(x, subjects, weights):
        import jax, jax.numpy as jnp
        import numpy as np
        B, C, D, T, N_SUBJECTS = (128, 64, 64, 512, 8)
        w = weights[subjects]
        out = jnp.einsum('bct,bcd->bdt', x, w)
        return out

    def _L1_cond_ref(x, conditions, weights):
        import jax, jax.numpy as jnp
        import numpy as np
        B, C, T = (128, 64, 512)
        S, D = (200, 64)
        w = weights[conditions]
        return jnp.einsum('bct,bcd->bdt', x, w)
    x = x + _L0_cond_ref(x, itok_B_0_7, L0_cond_weights)
    x = x + _L1_cond_ref(x, itok_B_1_198, L1_cond_weights)
    return x

_drawn_inputs = setup_inputs


def setup_inputs(seed=0):
    import zlib

    import numpy as np

    out = dict(_drawn_inputs(seed))
    spreads = {}
    factors = {}
    for name, (base, spread) in spreads.items():
        noise = np.random.default_rng([zlib.crc32(name.encode()), seed]).standard_normal(out[name].shape)
        drawn = base * np.exp(spread * noise) if base else spread * noise
        out[name] = jnp.asarray(drawn.astype(out[name].dtype))
    for name, factor in factors.items():
        out[name] = (out[name] * factor).astype(out[name].dtype)
    return out
```

```python
import concourse.bass as bass
from concourse import mybir
from contextlib import ExitStack



def bass_cond_residual_kernel(
    nc: bass.Bass,
    x_dram: bass.AP,
    subject_dram: bass.AP,
    cond_dram: bass.AP,
    w0_dram: bass.AP,
    w1_dram: bass.AP,
    out_dram: bass.AP,
):
    fp32 = mybir.dt.float32
    i32 = mybir.dt.int32
    ALU = mybir.AluOpType

    B, C, T = x_dram.shape
    S0 = w0_dram.shape[0]
    P = 2 * C
    PAIRS = B // 2
    BANK = 512
    GROUP = BANK // C
    GROUPS = PAIRS // GROUP
    RING = 2
    CHUNK = 4
    LANES = 4
    CHUNKS = PAIRS // CHUNK
    TILE = 2
    TILES = GROUP // TILE
    ITER = RING * GROUP
    TURNS = PAIRS // ITER
    assert ITER == LANES * CHUNK and B == P and T == BANK
    TWICE_V = 5 * C // 8
    HALVES = [slice(0, C), slice(C, P)]

    x_view = x_dram.rearrange("(p h) c t -> (h c) p t", h=2)
    out_view = out_dram.rearrange("(p h) c t -> (h c) p t", h=2)

    ctx = ExitStack()
    with ctx:
        def sb(name, shape, dt):
            return ctx.enter_context(nc.sbuf_tensor(name, shape, dt))

        def sem(name):
            return ctx.enter_context(nc.semaphore(name))

        xy = sb("xy", [P, PAIRS, T], fp32)
        w1_rows = xy[:, PAIRS - ITER:PAIRS, :].rearrange("b (two p) (q e) -> b two (p q) e", two=2, e=C)
        w1 = sb("w1", [P, PAIRS, C], fp32)
        w0_table = w1[0:S0, :, :]
        w0t = sb("w0t", [P, PAIRS, C], fp32)
        w0t_diag = sb("w0t_diag", [P, RING, GROUP, P], fp32)
        m_diag = sb("m_diag", [P, RING, GROUP, P], fp32)
        ident = sb("ident", [P, P], fp32)
        cond = sb("cond", [B, 1], i32)
        subjects = sb("subjects", [S0, B], i32)
        subject_id = sb("subject_id", [S0, 1], i32)
        one_hot = sb("one_hot", [S0, 2, PAIRS], fp32)

        psum = ctx.enter_context(nc.psum_tensor("psum", [P, 8, BANK], fp32))
        y_psum = psum[:, 0:RING * TILE, :].rearrange("q (r t) n -> q r t n", r=RING)
        m_psum = psum[:, RING * TILE:RING * TILE + RING, :].rearrange("q r (p e) -> q r p e", e=C)

        s_cond = sem("s_cond")
        s_subjects = sem("s_subjects")
        s_table = sem("s_table")
        s_gather = sem("s_gather")
        s_zeros = sem("s_zeros")
        s_ident = sem("s_ident")
        s_subject_id = sem("s_subject_id")
        s_diag_clear = sem("s_diag_clear")
        s_one_hot = sem("s_one_hot")
        s_w1_plus = sem("s_w1_plus")
        s_w1_twice_v = sem("s_w1_twice_v")
        s_w1_twice_s = sem("s_w1_twice_s")
        s_w0_picked = sem("s_w0_picked")
        s_w0_out_v = sem("s_w0_out_v")
        s_w0_out_s = sem("s_w0_out_s")
        s_w1_turned = sem("s_w1_turned")
        s_w1_out_v = sem("s_w1_out_v")
        s_w1_out_s = sem("s_w1_out_s")
        s_w0_diag = sem("s_w0_diag")
        s_m_psum = sem("s_m_psum")
        s_m = sem("s_m")
        s_y_psum = sem("s_y_psum")
        s_y_v = sem("s_y_v")
        s_y_s = sem("s_y_s")
        s_x = [sem(f"s_x{n}") for n in range(LANES)]
        s_out = [sem(f"s_out{n}") for n in range(LANES)]

        block = ctx.enter_context(nc.Block())

        @block.sync
        def _(sp):
            sp.dma_start(cond[:, :], cond_dram.rearrange("(b o) -> b o", o=1)).then_inc(s_cond, 16)
            sp.dma_start(subjects[:, :], subject_dram.rearrange("(o b) -> o b", o=1).to_broadcast((S0, B))
                         ).then_inc(s_subjects, 16)
            sp.dma_start(w0_table, w0_dram).then_inc(s_table, 16)

            for n in range(LANES):
                sp.dma_start(xy[:, n * CHUNK:(n + 1) * CHUNK, :],
                             x_view[:, n * CHUNK:(n + 1) * CHUNK, :]).then_inc(s_x[n], 16)
            def load(i):
                for n in range(LANES):
                    chunk = bass.ds(i * ITER + n * CHUNK, CHUNK)
                    sp.wait_ge(s_x[n], 16 * i)
                    sp.dma_start(xy[:, chunk, :], x_view[:, chunk, :]).then_inc(s_x[n], 16)

            with sp.Fori(1, TURNS - 1) as i:
                load(i)
            sp.wait_ge(s_w1_turned, 8)
            load(TURNS - 1)

            with sp.Fori(0, TURNS) as i:
                landed = 16 * i
                for n in range(LANES):
                    copied = sp.snap(sp.to_reg(i * LANES + (n + 1)))
                    chunk = bass.ds(i * ITER + n * CHUNK, CHUNK)
                    sp.wait_ge(s_out[n], landed)
                    sp.wait_ge(s_y_v, copied)
                    sp.wait_ge(s_y_s, copied)
                    sp.dma_start(out_view[:, chunk, :], xy[:, chunk, :]).then_inc(s_out[n], 16)
            for n in range(LANES):
                sp.wait_ge(s_out[n], 16 * TURNS)

        @block.gpsimd
        def _(pool):
            nc.gpsimd.iota(subject_id[:, :], pattern=[[0, 1]], base=0, channel_multiplier=1
                           ).then_inc(s_subject_id, 1)
            nc.gpsimd.memset(ident[:, :], 0.0).then_inc(s_zeros, 1)
            pool.wait_ge(s_cond, 16)
            nc.gpsimd.indirect_dma_start(
                out=w1_rows[:, 0, :, :].rearrange("b d e -> b (d e)"), out_offset=None,
                in_=w1_dram.rearrange("s d e -> s (d e)"),
                in_offset=bass.IndirectOffsetOnAxis(ap=cond[:, 0:1], axis=0)).then_inc(s_gather, 16)
            pool.wait_ge(s_zeros, 1)
            nc.gpsimd.affine_select(out=ident[:, :], in_=ident[:, :], compare_op=ALU.not_equal, fill=1.0,
                                    base=0, pattern=[[-1, P]], channel_multiplier=1).then_inc(s_ident, 1)

            pool.wait_ge(s_diag_clear, 2)
            pool.wait_ge(s_ident, 1)
            pool.wait_ge(s_w0_out_v, 4)
            pool.wait_ge(s_w0_out_s, 4)
            with pool.Fori(0, TURNS) as i:
                pool.wait_ge(s_m_psum, RING * i)
                for r in range(RING):
                    for h, rows in enumerate(HALVES):
                        nc.gpsimd.tensor_copy(
                            w0t_diag[rows, r, :, h * C:(h + 1) * C],
                            w0t[rows, bass.ds(i * ITER + r * GROUP, GROUP), :]).then_inc(s_w0_diag, 1)

        @block.tensor
        def _(pe):

            pe.wait_ge(s_table, 16)
            pe.wait_ge(s_one_hot, 1)
            for c in range(C):
                for h, rows in enumerate(HALVES):
                    last = nc.tensor.matmul(psum[rows, c // GROUP, (c % GROUP) * PAIRS:(c % GROUP + 1) * PAIRS],
                                            w0_table[:, c, :], one_hot[:, h, :], start=True, stop=True)
                if c % GROUP == GROUP - 1:
                    last.then_inc(s_w0_picked, 1)

            pe.wait_ge(s_ident, 1)
            pe.wait_ge(s_w1_twice_v, 1)
            pe.wait_ge(s_w1_twice_s, 1)
            for e in range(C):
                if e % 8 == 0:
                    if e < 32:
                        pe.wait_ge(s_w0_out_v, e // 8 + 1)
                        pe.wait_ge(s_w0_out_s, e // 8 + 1)
                    else:
                        pe.wait_ge(s_w1_out_v, e // 8 - 3)
                        pe.wait_ge(s_w1_out_s, e // 8 - 3)
                b = e // 4 % 8
                last = nc.tensor.transpose(
                    psum[:, b, (e % 4) * B:(e % 4 + 1) * B],
                    w1_rows[:, :, :, e].rearrange("b two d -> b (two d)"), ident[:, :])
                if e % 8 == 7:
                    last.then_inc(s_w1_turned, 1)

            def products(w1_first, r):
                for k in range(GROUP):
                    last = nc.tensor.matmul(m_psum[:, r, k, :], w0t_diag[:, r, k, :], w1[:, w1_first(k), :],
                                            start=True, stop=True)
                last.then_inc(s_m_psum, 1)

            def apply(i, r):
                for t in range(TILES):
                    slot = t % RING
                    chunk = (r * TILES + t) // 2
                    if t % 2 == 0:
                        pe.wait_ge(s_x[chunk], 16 * (i + 1))
                    pe.wait_ge((s_y_v, s_y_s)[slot], (i * RING + r) * (TILES // 2) + t // 2)
                    for k in range(TILE):
                        pair = i * ITER + (r * GROUP + t * TILE + k)
                        last = nc.tensor.matmul(y_psum[:, slot, k, :], m_diag[:, r, t * TILE + k, :],
                                                xy[:, pair, :] if isinstance(pair, int) else
                                                xy[:, bass.ds(pair, 1), :].rearrange("q o t -> q (o t)"),
                                                start=True, stop=True)
                    last.then_inc(s_y_psum, 1)

            pe.wait_ge(s_w1_out_v, 8)
            pe.wait_ge(s_w1_out_s, 8)
            pe.wait_ge(s_w0_diag, 2)
            products(lambda k: k, 0)
            with pe.Fori(0, TURNS - 1) as i:
                pe.wait_ge(s_w0_diag, 2 * (i * RING + 2))
                pe.wait_ge(s_m, i * RING)
                products(lambda k: bass.ds(i * ITER + (GROUP + k), 1), 1)
                pe.wait_ge(s_m, i * RING + 1)
                apply(i, 0)
                pe.wait_ge(s_w0_diag, 2 * (i * RING + 3))
                products(lambda k: bass.ds(i * ITER + (ITER + k), 1), 0)
                pe.wait_ge(s_m, i * RING + 2)
                apply(i, 1)
            pe.wait_ge(s_w0_diag, 2 * GROUPS)
            products(lambda k: PAIRS - GROUP + k, 1)
            pe.wait_ge(s_m, GROUPS - 1)
            apply(TURNS - 1, 0)
            pe.wait_ge(s_m, GROUPS)
            apply(TURNS - 1, 1)

        def w0_out(c8):
            return (w0t[:, :, c8 * GROUP:(c8 + 1) * GROUP],
                    psum[:, c8, :].rearrange("q (c p) -> q p c", c=GROUP))

        def w1_out(n, h):
            b = 2 * n % 8
            return (w1[HALVES[h], :, 8 * n:8 * n + 8],
                    psum[HALVES[h], b:b + 2, :].rearrange("q z (e p h) -> q h p (z e)", e=4, h=2)[:, h, :, :])

        @block.vector
        def _(dve):
            nc.vector.memset(w0t_diag[:, :, :, :], 0.0).then_inc(s_diag_clear, 1)
            nc.vector.memset(m_diag[:, :, :, :], 0.0).then_inc(s_diag_clear, 1)
            dve.wait_ge(s_subjects, 16)
            dve.wait_ge(s_subject_id, 1)
            nc.vector.tensor_scalar(one_hot[:, :, :], subjects[:, :].rearrange("s (p h) -> s h p", h=2),
                                    subject_id[:, 0:1], None, ALU.is_equal).then_inc(s_one_hot, 1)

            def w0_copy(b):
                dve.wait_ge(s_w0_picked, b + 1)
                nc.vector.tensor_copy(*w0_out(b)).then_inc(s_w0_out_v, 1)

            w0_copy(0)
            w0_copy(2)
            dve.wait_ge(s_gather, 16)
            diagonal = w1_rows[:, 0, :, :].rearrange("b d e -> b (d e)")[:, ::C + 1]
            nc.vector.tensor_scalar_add(diagonal, diagonal, 1.0).then_inc(s_w1_plus, 1)
            dve.wait_ge(s_w1_plus, 1)
            nc.vector.tensor_copy(w1_rows[:, 1, 0:TWICE_V, :], w1_rows[:, 0, 0:TWICE_V, :]
                                  ).then_inc(s_w1_twice_v, 1)
            w0_copy(4)
            w0_copy(6)
            for n in range(8):
                dve.wait_ge(s_w1_turned, n + 1)
                nc.vector.tensor_copy(*w1_out(n, 0)).then_inc(s_w1_out_v, 1)

            def finish_m(first, r):
                for h, rows in enumerate(HALVES):
                    last = nc.vector.tensor_tensor(m_diag[rows, r, :, h * C:(h + 1) * C], m_psum[rows, r, :, :],
                                                   w1[rows, first, :], ALU.add)
                last.then_inc(s_m, 1)

            def copy_y(i, r):
                for t in range(0, TILES, 2):
                    dve.wait_ge(s_y_psum, (i * RING + r) * TILES + (t + 1))
                    nc.vector.tensor_copy(xy[:, bass.ds(i * ITER + (r * GROUP + t * TILE), TILE), :],
                                          y_psum[:, 0, :, :]).then_inc(s_y_v, 1)

            dve.wait_ge(s_w1_out_s, 8)
            dve.wait_ge(s_diag_clear, 2)
            dve.wait_ge(s_m_psum, 1)
            finish_m(slice(0, GROUP), 0)
            with dve.Fori(0, TURNS - 1) as i:
                dve.wait_ge(s_m_psum, i * RING + 2)
                dve.wait_ge(s_y_psum, i * RING * TILES)
                finish_m(bass.ds(i * ITER + GROUP, GROUP), 1)
                copy_y(i, 0)
                dve.wait_ge(s_m_psum, i * RING + 3)
                dve.wait_ge(s_y_psum, (i * RING + 1) * TILES)
                finish_m(bass.ds(i * ITER + ITER, GROUP), 0)
                copy_y(i, 1)
            dve.wait_ge(s_m_psum, GROUPS)
            dve.wait_ge(s_y_psum, (GROUPS - 2) * TILES)
            finish_m(slice(PAIRS - GROUP, PAIRS), 1)
            copy_y(TURNS - 1, 0)
            copy_y(TURNS - 1, 1)

        @block.scalar
        def _(act):
            def w0_copy(b):
                act.wait_ge(s_w0_picked, b + 1)
                nc.scalar.copy(*w0_out(b)).then_inc(s_w0_out_s, 1)

            w0_copy(1)
            w0_copy(3)
            act.wait_ge(s_w1_plus, 1)
            nc.scalar.copy(w1_rows[:, 1, TWICE_V:C, :], w1_rows[:, 0, TWICE_V:C, :]).then_inc(s_w1_twice_s, 1)
            w0_copy(5)
            w0_copy(7)
            for n in range(8):
                act.wait_ge(s_w1_turned, n + 1)
                nc.scalar.copy(*w1_out(n, 1)).then_inc(s_w1_out_s, 1)
            with act.Fori(0, TURNS) as i:
                for t in range(1, RING * TILES, 2):
                    act.wait_ge(s_y_psum, i * (RING * TILES) + (t + 1))
                    nc.scalar.copy(xy[:, bass.ds(i * ITER + t * TILE, TILE), :],
                                   y_psum[:, 1, :, :]).then_inc(s_y_s, 1)


_INS = ['x', 'itok_B_0_7', 'itok_B_1_198', 'L0_cond_weights', 'L1_cond_weights']
_OUTS = [((128, 64, 512), 'float32')]


def kernel(**inputs):
    import numpy as _np
    import concourse.bacc as _bacc
    from concourse import mybir as _mybir
    from concourse.bass_utils import run_bass_kernel_spmd as _run

    nc = _bacc.Bacc("TRN2", target_bir_lowering=False, num_devices=1)
    arrays, args = {}, []
    for name in _INS:
        a = _np.ascontiguousarray(inputs[name])
        arrays[f"in_{name}_dram"] = a
        args.append(nc.dram_tensor(f"in_{name}_dram", a.shape, _mybir.dt.from_np(a.dtype), kind="ExternalInput").ap())
    for i, (shape, dtype) in enumerate(_OUTS):
        dt = _mybir.dt.from_np(_np.dtype(dtype))
        args.append(nc.dram_tensor(f"out_{i}_dram", shape, dt, kind="ExternalOutput").ap())
    bass_cond_residual_kernel(nc, *args)
    r = _run(nc, [arrays], core_ids=[0])
    got = tuple(r.results[0][f"out_{i}_dram"] for i in range(len(_OUTS)))
    return got[0]
```

```python
import concourse.bass as bass
from concourse import mybir
from contextlib import ExitStack



def bass_cond_residual_kernel(
    nc: bass.Bass,
    x_dram: bass.AP,
    subject_dram: bass.AP,
    cond_dram: bass.AP,
    w0_dram: bass.AP,
    w1_dram: bass.AP,
    out_dram: bass.AP,
):
    fp32 = mybir.dt.float32
    i32 = mybir.dt.int32
    ALU = mybir.AluOpType

    B, C, T = x_dram.shape
    S0 = w0_dram.shape[0]
    P = 2 * C
    PAIRS = B // 2
    BANK = 512
    GROUP = BANK // C
    RING = 2
    CHUNK = 4
    LANES = 4
    TILE = 2
    TILES = GROUP // TILE
    ITER = RING * GROUP
    TURNS = PAIRS // ITER
    assert ITER == LANES * CHUNK and B == P and T == BANK
    ROWS = S0 * C // P
    W1_EACH = 2 * BANK // B
    W1_TURNS = C // W1_EACH
    POOL = mybir.EngineType.Pool
    HALVES = [slice(0, C), slice(C, P)]

    x_view = x_dram.rearrange("(p h) c t -> (h c) p t", h=2)
    out_view = out_dram.rearrange("(p h) c t -> (h c) p t", h=2)

    ctx = ExitStack()
    with ctx:
        def sb(name, shape, dt):
            return ctx.enter_context(nc.sbuf_tensor(name, shape, dt))

        def sem(name):
            return ctx.enter_context(nc.semaphore(name))

        xy = sb("xy", [P, PAIRS, T], fp32)
        w0_rows = sb("w0_rows", [P, ROWS, C], fp32)
        w0t = sb("w0t", [P, S0 * C], fp32)
        w1_rows = sb("w1_rows", [B, C, C], fp32)
        w1 = sb("w1", [P, PAIRS, C], fp32)
        w0t_diag = sb("w0t_diag", [P, RING, GROUP, P], fp32)
        m_diag = sb("m_diag", [P, RING, GROUP, P], fp32)
        ident = sb("ident", [P, P], fp32)
        cond = sb("cond", [B, 1], i32)
        subjects = sb("subjects", [1, B], i32)

        psum = ctx.enter_context(nc.psum_tensor("psum", [P, 8, BANK], fp32))
        y_psum = psum[:, 0:RING * TILE, :].rearrange("q (r t) n -> q r t n", r=RING)
        m_psum = psum[:, RING * TILE:RING * TILE + RING, :].rearrange("q r (p e) -> q r p e", e=C)
        w0_psum = psum[0:C, 7, :]
        W1_BANKS = 6

        s_cond = sem("s_cond")
        s_subjects = sem("s_subjects")
        s_w0_rows = sem("s_w0_rows")
        s_gather = sem("s_gather")
        s_gather_sent = sem("s_gather_sent")
        s_zeros = sem("s_zeros")
        s_ident = sem("s_ident")
        s_diag_clear = sem("s_diag_clear")
        s_w0_turned = sem("s_w0_turned")
        s_w0t = sem("s_w0t")
        s_w1_plus = sem("s_w1_plus")
        s_w1_turned = sem("s_w1_turned")
        s_w1_v = sem("s_w1_v")
        s_w1_s = sem("s_w1_s")
        s_w0_diag = sem("s_w0_diag")
        s_m_psum = sem("s_m_psum")
        s_m_v = sem("s_m_v")
        s_m_s = sem("s_m_s")
        s_y_psum = sem("s_y_psum")
        s_y_v = sem("s_y_v")
        s_y_s = sem("s_y_s")
        s_x = [sem(f"s_x{n}") for n in range(LANES)]
        s_out = [sem(f"s_out{n}") for n in range(LANES)]

        block = ctx.enter_context(nc.Block())


        @block.sync
        def _(sp):
            def load(i, n):
                chunk = bass.ds(i * ITER + n * CHUNK, CHUNK)
                sp.dma_start(xy[:, chunk, :], x_view[:, chunk, :]).then_inc(s_x[n], 16)

            def store(i, n):
                chunk = bass.ds(i * ITER + n * CHUNK, CHUNK)
                sp.dma_start(out_view[:, chunk, :], xy[:, chunk, :]).then_inc(s_out[n], 16)

            sp.dma_start(cond[:, :], cond_dram.rearrange("(b o) -> b o", o=1)).then_inc(s_cond, 16)
            load(0, 0)
            sp.dma_start(w0_rows[:, :, :], w0_dram.rearrange("s (k j) d -> (s k) j d", j=ROWS)
                         ).then_inc(s_w0_rows, 16)
            sp.dma_start(subjects[:, :], subject_dram.rearrange("(o b) -> o b", o=1)).then_inc(s_subjects, 16)
            sp.wait_ge(s_gather_sent, 1)
            for n in range(1, LANES):
                load(0, n)
            with sp.Fori(1, TURNS) as i:
                for n in range(LANES):
                    sp.wait_ge(s_x[n], 16 * i)
                    load(i, n)

            for n in range(LANES):
                sp.wait_ge(s_y_v, n + 1)
                sp.wait_ge(s_y_s, n + 1)
                store(0, n)
            with sp.Fori(1, TURNS) as i:
                landed = sp.snap(sp.to_reg(16 * i))
                for n in range(LANES):
                    copied = sp.snap(sp.to_reg(i * LANES + (n + 1)))
                    sp.wait_ge(s_y_v, copied)
                    sp.wait_ge(s_y_s, copied)
                    sp.wait_ge(s_out[n], landed)
                    store(i, n)
            for n in range(LANES):
                sp.wait_ge(s_out[n], 16 * TURNS)

        @block.gpsimd
        def _(pool):
            nc.gpsimd.memset(ident[:, :], 0.0).then_inc(s_zeros, 1)
            pool.wait_ge(s_zeros, 1)
            nc.gpsimd.affine_select(out=ident[:, :], in_=ident[:, :], compare_op=ALU.not_equal, fill=1.0,
                                    base=0, pattern=[[-1, P]], channel_multiplier=1).then_inc(s_ident, 1)
            pool.wait_ge(s_cond, 16)
            nc.gpsimd.indirect_dma_start(
                out=w1_rows[:, :, :].rearrange("b d e -> b (d e)"), out_offset=None,
                in_=w1_dram.rearrange("s d e -> s (d e)"),
                in_offset=bass.IndirectOffsetOnAxis(ap=cond[:, 0:1], axis=0),
                engine_sem=s_gather_sent).then_inc(s_gather, 16)

            def spread(i):
                for r in range(RING):
                    first = i * (2 * ITER) + r * (2 * GROUP)
                    _, picked = nc.values_load_multi_w_load_instructions(
                        subjects[0:1, bass.ds(first, 2 * GROUP)], engines=(POOL,), min_val=0, max_val=S0 - 1,
                        skip_runtime_bounds_check_because="subjects index the 8 matrices")
                    for n in range(2 * GROUP):
                        h, rows = n % 2, HALVES[n % 2]
                        nc.gpsimd.tensor_copy(w0t_diag[rows, r, n // 2, h * C:(h + 1) * C],
                                              w0t[rows, bass.ds(picked[n] * C, C)]).then_inc(s_w0_diag, 1)

            pool.wait_ge(s_ident, 1)
            pool.wait_ge(s_gather, 16)
            pool.wait_ge(s_subjects, 16)
            pool.wait_ge(s_diag_clear, 1)
            pool.wait_ge(s_w0t, 2)
            spread(0)
            with pool.Fori(1, TURNS) as i:
                pool.wait_ge(s_m_psum, RING * i)
                spread(i)

        @block.tensor
        def _(pe):
            pe.wait_ge(s_ident, 1)
            pe.wait_ge(s_w0_rows, 16)
            for j in range(ROWS):
                last = nc.tensor.transpose(w0_psum[:, j * P:(j + 1) * P], w0_rows[:, j, :], ident[:, :])
            last.then_inc(s_w0_turned, 1)

            pe.wait_ge(s_w1_plus, 1)
            for e in range(C):
                n = e // W1_EACH
                if e % W1_EACH == 0 and n >= W1_BANKS // 2:
                    before = n - W1_BANKS // 2
                    pe.wait_ge((s_w1_v, s_w1_s)[before % 2], before // 2 + 1)
                bank = 2 * n % W1_BANKS + e % W1_EACH // 4
                last = nc.tensor.transpose(psum[0:C, bank, (e % 4) * B:(e % 4 + 1) * B],
                                           w1_rows[:, :, e], ident[:, :])
                if e % W1_EACH == W1_EACH - 1:
                    last.then_inc(s_w1_turned, 1)

            def products(first, r):
                for k in range(GROUP):
                    last = nc.tensor.matmul(m_psum[:, r, k, :], w0t_diag[:, r, k, :],
                                            w1[:, bass.ds(first + k, 1), :].rearrange("q o e -> q (o e)"),
                                            start=True, stop=True)
                last.then_inc(s_m_psum, 1)

            def apply(i, r):
                for t in range(TILES):
                    slot = t % RING
                    if t % 2 == 0:
                        pe.wait_ge(s_x[(r * TILES + t) // 2], 16 * i + 16)
                    before = i * LANES + (r * (TILES // 2) + t // 2)
                    if not (isinstance(before, int) and before == 0):
                        pe.wait_ge((s_y_v, s_y_s)[slot], before)
                    for k in range(TILE):
                        pair = bass.ds(i * ITER + (r * GROUP + t * TILE + k), 1)
                        last = nc.tensor.matmul(y_psum[:, slot, k, :], m_diag[:, r, t * TILE + k, :],
                                                xy[:, pair, :].rearrange("q o t -> q (o t)"),
                                                start=True, stop=True)
                    last.then_inc(s_y_psum, 1)

            def group(i, r, following=True):
                if following:
                    pe.wait_ge(s_w0_diag, i * (2 * ITER) + 2 * GROUP * (r + 2))
                    products(i * ITER + (r + 1) * GROUP, 1 - r)
                pe.wait_ge(s_m_v, i * RING + (r + 1))
                pe.wait_ge(s_m_s, i * RING + (r + 1))
                apply(i, r)

            pe.wait_ge(s_w1_v, W1_TURNS // 2)
            pe.wait_ge(s_w1_s, W1_TURNS // 2)
            pe.wait_ge(s_w0_diag, 2 * GROUP)
            products(0, 0)
            group(0, 0)
            group(0, 1)
            with pe.Fori(1, TURNS - 1) as i:
                group(i, 0)
                group(i, 1)
            group(TURNS - 1, 0)
            group(TURNS - 1, 1, following=False)


        def copy_w1(eng, copy, done, n):
            eng.wait_ge(s_w1_turned, n + 1)
            bank = 2 * n % W1_BANKS
            for h, rows in enumerate(HALVES):
                last = copy(w1[rows, :, W1_EACH * n:W1_EACH * (n + 1)],
                            psum[0:C, bank:bank + 2, :].rearrange("q z (e p h) -> q h p (z e)", h=2, e=4)[:, h, :, :])
            last.then_inc(done, 1)

        def copy_m(eng, copy, done, h, i, r):
            eng.wait_ge(s_m_psum, i * RING + (r + 1))
            before = i * (RING * TILES) + (r - 1) * TILES
            if not (isinstance(before, int) and before <= 0):
                eng.wait_ge(s_y_psum, before)
            copy(m_diag[HALVES[h], r, :, h * C:(h + 1) * C], m_psum[HALVES[h], r, :, :]).then_inc(done, 1)

        def copy_y(eng, copy, done, slot, i, r):
            for t in range(slot, TILES, RING):
                eng.wait_ge(s_y_psum, i * (RING * TILES) + (r * TILES + t + 1))
                copy(xy[:, bass.ds(i * ITER + (r * GROUP + t * TILE), TILE), :],
                     y_psum[:, slot, :, :]).then_inc(done, 1)

        def main_part(eng, copy, m_done, y_done, half):
            def turn(i, last=False):
                copy_m(eng, copy, m_done, half, i, 1)
                copy_y(eng, copy, y_done, half, i, 0)
                if not last:
                    copy_m(eng, copy, m_done, half, i + 1, 0)
                copy_y(eng, copy, y_done, half, i, 1)

            copy_m(eng, copy, m_done, half, 0, 0)
            turn(0)
            with eng.Fori(1, TURNS - 1) as i:
                turn(i)
            turn(TURNS - 1, last=True)

        @block.vector
        def _(dve):
            nc.vector.memset(w0t_diag[:, :, :, :], 0.0).then_inc(s_diag_clear, 1)
            dve.wait_ge(s_ident, 1)
            dve.wait_ge(s_w0_turned, 1)
            for rows in HALVES:
                nc.vector.tensor_tensor(
                    w0t[rows, :].rearrange("q (s k j) -> q s k j", s=S0, j=ROWS),
                    w0_psum.rearrange("q (j s k) -> q s k j", s=S0, j=ROWS),
                    ident[0:C, 0:C].rearrange("q (o k j) -> q o k j", o=1, j=ROWS
                                              ).to_broadcast((C, S0, C // ROWS, ROWS)), ALU.add).then_inc(s_w0t, 1)
            nc.vector.memset(m_diag[:, :, :, :], 0.0).then_inc(s_diag_clear, 1)
            dve.wait_ge(s_gather, 16)
            diagonal = w1_rows[:, :, :].rearrange("b d e -> b (d e)")[:, ::C + 1]
            nc.vector.tensor_scalar_add(diagonal, diagonal, 1.0).then_inc(s_w1_plus, 1)
            for n in range(0, W1_TURNS, 2):
                copy_w1(dve, nc.vector.tensor_copy, s_w1_v, n)
            dve.wait_ge(s_diag_clear, 2)
            main_part(dve, nc.vector.tensor_copy, s_m_v, s_y_v, 0)

        @block.scalar
        def _(act):
            for n in range(1, W1_TURNS, 2):
                copy_w1(act, nc.scalar.copy, s_w1_s, n)
            act.wait_ge(s_diag_clear, 2)
            main_part(act, nc.scalar.copy, s_m_s, s_y_s, 1)


_INS = ['x', 'itok_B_0_7', 'itok_B_1_198', 'L0_cond_weights', 'L1_cond_weights']
_OUTS = [((128, 64, 512), 'float32')]


def kernel(**inputs):
    import numpy as _np
    import concourse.bacc as _bacc
    from concourse import mybir as _mybir
    from concourse.bass_utils import run_bass_kernel_spmd as _run

    nc = _bacc.Bacc("TRN2", target_bir_lowering=False, num_devices=1)
    arrays, args = {}, []
    for name in _INS:
        a = _np.ascontiguousarray(inputs[name])
        arrays[f"in_{name}_dram"] = a
        args.append(nc.dram_tensor(f"in_{name}_dram", a.shape, _mybir.dt.from_np(a.dtype), kind="ExternalInput").ap())
    for i, (shape, dtype) in enumerate(_OUTS):
        dt = _mybir.dt.from_np(_np.dtype(dtype))
        args.append(nc.dram_tensor(f"out_{i}_dram", shape, dt, kind="ExternalOutput").ap())
    bass_cond_residual_kernel(nc, *args)
    r = _run(nc, [arrays], core_ids=[0])
    got = tuple(r.results[0][f"out_{i}_dram"] for i in range(len(_OUTS)))
    return got[0]
```
